# Optimizing a Trainium2 kernel written in Bass

```python
import numpy as np
import jax
import jax.numpy as jnp

def _softmax(x, axis=-1):
    return jax.nn.softmax(x, axis=axis)

def _gelu(x):
    return jax.nn.gelu(x, approximate=True)

def _silu(x):
    return jax.nn.silu(x)

def _sigmoid(x):
    return jax.nn.sigmoid(x)

def _layernorm(x, axis=-1, eps=1e-05):
    m = jnp.mean(x, axis=axis, keepdims=True)
    v = jnp.var(x, axis=axis, keepdims=True)
    return (x - m) / jnp.sqrt(v + eps)

def _scatter_add(tgt, idx, src, axis=0):
    return tgt.at[idx].add(src)

def _segment_sum(src, seg, n):
    return jax.ops.segment_sum(src, seg, n)
kernel_name = 'mk_rec_standalone_d1_rec_r8_0e164e'

def setup_inputs(seed: int=0):
    np.random.seed(seed)
    _w = jnp.asarray

    def _rec_inputs():
        import jax
        import jax.numpy as jnp
        _rk = jax.random.key(seed)
        r_Xi = jax.random.randint(jax.random.fold_in(_rk, 1), (2048, 26, 1), 0, 12500, jnp.int32)
        r_title_feature = jnp.stack([jax.random.randint(jax.random.fold_in(jax.random.fold_in(_rk, 2), 0), (2048,), 5, 49997, jnp.int32), jax.random.randint(jax.random.fold_in(jax.random.fold_in(_rk, 2), 1), (2048,), 3, 49998, jnp.int32), jax.random.randint(jax.random.fold_in(jax.random.fold_in(_rk, 2), 2), (2048,), 7, 6250, jnp.int32), jax.random.randint(jax.random.fold_in(jax.random.fold_in(_rk, 2), 3), (2048,), 3, 49997, jnp.int32), jax.random.randint(jax.random.fold_in(jax.random.fold_in(_rk, 2), 4), (2048,), 4, 49998, jnp.int32), jax.random.randint(jax.random.fold_in(jax.random.fold_in(_rk, 2), 5), (2048,), 2, 6250, jnp.int32), jax.random.randint(jax.random.fold_in(jax.random.fold_in(_rk, 2), 6), (2048,), 2, 6250, jnp.int32), jax.random.randint(jax.random.fold_in(jax.random.fold_in(_rk, 2), 7), (2048,), 5, 49983, jnp.int32), jax.random.randint(jax.random.fold_in(jax.random.fold_in(_rk, 2), 8), (2048,), 2, 6250, jnp.int32), jax.random.randint(jax.random.fold_in(jax.random.fold_in(_rk, 2), 9), (2048,), 0, 49994, jnp.int32), jax.random.randint(jax.random.fold_in(jax.random.fold_in(_rk, 2), 10), (2048,), 5, 6250, jnp.int32), jax.random.randint(jax.random.fold_in(jax.random.fold_in(_rk, 2), 11), (2048,), 2, 49998, jnp.int32), jax.random.randint(jax.random.fold_in(jax.random.fold_in(_rk, 2), 12), (2048,), 3, 49990, jnp.int32), jax.random.randint(jax.random.fold_in(jax.random.fold_in(_rk, 2), 13), (2048,), 1, 49995, jnp.int32), jax.random.randint(jax.random.fold_in(jax.random.fold_in(_rk, 2), 14), (2048,), 0, 6250, jnp.int32), jax.random.randint(jax.random.fold_in(jax.random.fold_in(_rk, 2), 15), (2048,), 0, 6250, jnp.int32), jax.random.randint(jax.random.fold_in(jax.random.fold_in(_rk, 2), 16), (2048,), 5, 49986, jnp.int32), jax.random.randint(jax.random.fold_in(jax.random.fold_in(_rk, 2), 17), (2048,), 0, 49998, jnp.int32), jax.random.randint(jax.random.fold_in(jax.random.fold_in(_rk, 2), 18), (2048,), 0, 49998, jnp.int32), jax.random.randint(jax.random.fold_in(jax.random.fold_in(_rk, 2), 19), (2048,), 6, 6250, jnp.int32)], axis=1)
        return (r_Xi, r_title_feature)
    r_Xi, r_title_feature = _rec_inputs()

    def _L0_rec_setup():
        import jax, jax.numpy as jnp
        import numpy as np
        B = 2048
        F = 26
        V = 12500
        E = 32
        VT = 6250
        L = 20
        DVF = 128
        H1, H2 = (512, 256)
        key = jax.random.key(seed)
        ks = jax.random.split(key, 16)
        inp = {'Xi': jax.random.randint(ks[0], (B, F, 1), 0, V), 'Xv': jax.random.uniform(ks[1], (B, F), dtype=jnp.float32), 'video_feature': jax.random.normal(ks[2], (B, DVF), dtype=jnp.float32), 'title_feature': jax.random.randint(ks[3], (B, L), 0, VT), 'title_value': jax.random.uniform(ks[4], (B, L), dtype=jnp.float32), 'first_tables': jax.random.normal(ks[5], (F, V), dtype=jnp.float32) * 0.01, 'second_tables': jax.random.normal(ks[6], (F, V, E), dtype=jnp.float32) * 0.01, 'title_table': jax.random.normal(ks[7], (VT, E), dtype=jnp.float32) * 0.01, 'video_W': jax.random.normal(ks[8], (E, DVF), dtype=jnp.float32) * (1.0 / np.sqrt(DVF)), 'video_b': jnp.zeros((E,), dtype=jnp.float32), 'W1': jax.random.normal(ks[9], ((F + 2) * E, H1), dtype=jnp.float32) * (1.0 / np.sqrt((F + 2) * E)), 'b1': jnp.zeros((H1,), dtype=jnp.float32), 'W2': jax.random.normal(ks[10], (H1, H2), dtype=jnp.float32) * (1.0 / np.sqrt(H1)), 'b2': jnp.zeros((H2,), dtype=jnp.float32), 'bias': jax.random.normal(ks[11], (1,), dtype=jnp.float32)}
        return inp
    _L0_rec_all = _L0_rec_setup()
    _L0_rec_in = {k: v for k, v in _L0_rec_all.items() if k in ('Xv', 'video_feature', 'title_value', 'first_tables', 'second_tables', 'title_table', 'video_W', 'video_b', 'W1', 'b1', 'W2', 'b2', 'bias')}
    del _L0_rec_all
    return {'r_Xi': r_Xi, 'r_title_feature': r_title_feature, 'L0_rec_Xv': _L0_rec_in['Xv'], 'L0_rec_video_feature': _L0_rec_in['video_feature'], 'L0_rec_title_value': _L0_rec_in['title_value'], 'L0_rec_first_tables': _L0_rec_in['first_tables'], 'L0_rec_second_tables': _L0_rec_in['second_tables'], 'L0_rec_title_table': _L0_rec_in['title_table'], 'L0_rec_video_W': _L0_rec_in['video_W'], 'L0_rec_video_b': _L0_rec_in['video_b'], 'L0_rec_W1': _L0_rec_in['W1'], 'L0_rec_b1': _L0_rec_in['b1'], 'L0_rec_W2': _L0_rec_in['W2'], 'L0_rec_b2': _L0_rec_in['b2'], 'L0_rec_bias': _L0_rec_in['bias']}

def reference(r_Xi, r_title_feature, L0_rec_Xv, L0_rec_video_feature, L0_rec_title_value, L0_rec_first_tables, L0_rec_second_tables, L0_rec_title_table, L0_rec_video_W, L0_rec_video_b, L0_rec_W1, L0_rec_b1, L0_rec_W2, L0_rec_b2, L0_rec_bias):
    import jax
    import jax.numpy as jnp

    def _L0_rec_ref(Xi, Xv, video_feature, title_feature, title_value, first_tables, second_tables, title_table, video_W, video_b, W1, b1, W2, b2, bias):
        import jax, jax.numpy as jnp
        import numpy as np
        B = 2048
        F = 26
        V = 12500
        E = 32
        VT = 6250
        L = 20
        DVF = 128
        H1, H2 = (512, 256)
        idx = Xi[:, :, 0]
        f_idx = jnp.arange(F)[None, :]
        fm_first_order = first_tables[f_idx, idx] * Xv
        emb = second_tables[f_idx, idx] * Xv[:, :, None]
        sum_emb = jnp.sum(emb, axis=1)
        sum_sq = sum_emb * sum_emb
        sq_sum = jnp.sum(emb * emb, axis=1)
        fm_second_order = 0.5 * (sum_sq - sq_sum)
        title_emb = jnp.sum(title_table[title_feature] * title_value[:, :, None], axis=1)
        video_emb = video_feature @ video_W.T + video_b
        deep_emb = jnp.concatenate([emb.reshape(B, F * E), title_emb, video_emb], axis=1)
        x = jax.nn.relu(deep_emb @ W1 + b1)
        x = jax.nn.relu(x @ W2 + b2)
        total = jnp.sum(fm_first_order, axis=1) + jnp.sum(fm_second_order, axis=1) + jnp.sum(x, axis=1) + bias[0]
        return total
    y = _L0_rec_ref(r_Xi, L0_rec_Xv, L0_rec_video_feature, r_title_feature, L0_rec_title_value, L0_rec_first_tables, L0_rec_second_tables, L0_rec_title_table, L0_rec_video_W, L0_rec_video_b, L0_rec_W1, L0_rec_b1, L0_rec_W2, L0_rec_b2, L0_rec_bias)
    return y

_drawn_inputs = setup_inputs


def setup_inputs(seed=0):
    import zlib

    import numpy as np

    out = dict(_drawn_inputs(seed))
    spreads = {'L0_rec_video_b': (0.0, 2.0), 'L0_rec_b1': (0.0, 0.691), 'L0_rec_b2': (0.0, 0.506)}
    factors = {'L0_rec_Xv': 8.0,
     'L0_rec_title_value': 8.0,
     'L0_rec_first_tables': 8.0,
     'L0_rec_second_tables': 8.0,
     'L0_rec_title_table': 8.0,
     'L0_rec_video_feature': 3.174,
     'L0_rec_video_W': 3.095}
    for name, (base, spread) in spreads.items():
        noise = np.random.default_rng([zlib.crc32(name.encode()), seed]).standard_normal(out[name].shape)
        drawn = base * np.exp(spread * noise) if base else spread * noise
        out[name] = jnp.asarray(drawn.astype(out[name].dtype))
    for name, factor in factors.items():
        out[name] = (out[name] * factor).astype(out[name].dtype)
    return out
```

```python
from contextlib import ExitStack

import concourse.bass as bass
from concourse import mybir

B = 2048
F = 26
V = 12500
E = 32
EA = E + 1
VT = 6250
L = 20
DVF = 128
H1, H2 = 512, 256
P = 128
TILES = B // P
PAIRS = TILES // 2
FPB = P // E
KB = (F + 2) * E // P
LAST = (F + 1) * E - (KB - 1) * P
KH = H1 // P
K2 = H2 // P
VCHUNK = 512


def build(nc, table, title_table, field_index, field_value, title_index, title_value, video_t, video_wt,
          video_b, w1, b1, w2, b2, bias, field_base, identity, out):
    fp32, i32 = mybir.dt.float32, mybir.dt.int32
    ALU = mybir.AluOpType
    ACT = mybir.ActivationFunctionType
    AXX = mybir.AxisListType.X
    ctx = ExitStack()
    with ctx:
        def sb(name, shape, dt=fp32):
            return ctx.enter_context(nc.sbuf_tensor(name, shape, dt))

        def ps(name, shape):
            return ctx.enter_context(nc.psum_tensor(name, shape, fp32))

        def sem(name):
            return ctx.enter_context(nc.semaphore(name))

        findex = sb("findex", [P, TILES, F], i32)
        tindex = sb("tindex", [P, TILES, L], i32)
        fvalue = sb("fvalue", [P, TILES, F])
        tvalue = sb("tvalue", [P, TILES, L])
        fbase = sb("fbase", [P, F], i32)
        ident = sb("ident", [P, P])
        video_sb = sb("video_sb", [P, B])
        vwt_sb = sb("vwt_sb", [P, E])
        vb_sb = sb("vb_sb", [P, 1])
        w1_sb = sb("w1_sb", [P, KB, H1])
        w2_sb = sb("w2_sb", [P, KH, H2])
        b1_sb = sb("b1_sb", [P, KH])
        b2_sb = sb("b2_sb", [P, K2])
        bias_sb = sb("bias_sb", [P, 1])
        ones = sb("ones", [P, 1])
        fneg = sb("fneg", [P, F])
        tneg = sb("tneg", [P, L])
        fslot = [sb(f"fslot{s}", [P, F], i32) for s in range(2)]
        tslot = [sb(f"tslot{s}", [P, L], i32) for s in range(2)]
        rows = [sb(f"rows{s}", [P, F, EA]) for s in range(2)]
        words = [sb(f"words{s}", [P, L, E]) for s in range(2)]
        scaled = [sb(f"scaled{s}", [P, F + 1, E]) for s in range(2)]
        wscaled = sb("wscaled", [P, L, E])
        fieldsum = [sb(f"fieldsum{s}", [P, E]) for s in range(2)]
        weighted = sb("weighted", [P, F])
        square = sb("square", [P, F, E])
        square_s = sb("square_s", [P, E])
        sq_of_sum = sb("sq_of_sum", [P, TILES])
        sum_of_sq = sb("sum_of_sq", [P, TILES])
        first = sb("first", [P, TILES])
        deep = sb("deep", [P, TILES])
        diff = sb("diff", [P, TILES])
        linear = sb("linear", [P, TILES])
        total = sb("total", [P, TILES])
        video_emb = sb("video_emb", [P, B])
        xt = [sb(f"xt{s}", [P, KB, P]) for s in range(2)]
        h1 = [sb(f"h1{s}", [P, KH, P]) for s in range(2)]
        h2 = [sb(f"h2{s}", [P, K2, P]) for s in range(2)]

        pt = [ps("pt0", [P, FPB, P]), ps("pt1", [P, FPB, P])]
        ph1 = ps("ph1", [P, KH, P])
        ph2 = ps("ph2", [P, FPB, P])
        py = ps("py", [P, VCHUNK])
        pv = ps("pv", [P, VCHUNK])

        index_loaded = sem("index_loaded")
        values_loaded = sem("values_loaded")
        weights_loaded = sem("weights_loaded")
        video_loaded = sem("video_loaded")
        index_step = sem("index_step")
        index_ready = sem("index_ready")
        gathers_begun = sem("gathers_begun")
        gathered = [sem(f"gathered{s}") for s in range(2)]
        rows_used = sem("rows_used")
        wscaled_ready = sem("wscaled_ready")
        sums_ready = sem("sums_ready")
        squared = sem("squared")
        transposed = sem("transposed")
        ones_ready = sem("ones_ready")
        xt_ready = sem("xt_ready")
        h1_summed = sem("h1_summed")
        h1_ready = sem("h1_ready")
        h2_summed = sem("h2_summed")
        h2_ready = sem("h2_ready")
        y_summed = sem("y_summed")
        deep_ready = sem("deep_ready")
        video_summed = sem("video_summed")
        video_ready = sem("video_ready")
        total_step = sem("total_step")
        out_written = sem("out_written")
        block = ctx.enter_context(nc.Block())

        @block.sync
        def _(sp):
            sp.dma_start(findex[:], field_index).then_inc(index_loaded, 16)
            sp.dma_start(fbase[:], field_base).then_inc(index_loaded, 16)
            sp.dma_start(tindex[:], title_index).then_inc(index_loaded, 16)
            sp.dma_start(fvalue[:], field_value).then_inc(values_loaded, 16)
            sp.dma_start(tvalue[:], title_value).then_inc(values_loaded, 16)
            sp.dma_start(video_sb[:], video_t).then_inc(video_loaded, 16)
            sp.dma_start(vwt_sb[:], video_wt).then_inc(video_loaded, 16)
            sp.dma_start(vb_sb[LAST:P, :], video_b).then_inc(video_loaded, 16)
            sp.dma_start(ident[:], identity).then_inc(weights_loaded, 16)
            sp.dma_start(w1_sb[:], w1.rearrange("(k p) n -> p k n", p=P)).then_inc(weights_loaded, 16)
            sp.dma_start(w2_sb[:], w2.rearrange("(k p) n -> p k n", p=P)).then_inc(weights_loaded, 16)
            sp.dma_start(b1_sb[:], b1).then_inc(weights_loaded, 16)
            sp.dma_start(b2_sb[:], b2).then_inc(weights_loaded, 16)
            sp.dma_start(bias_sb[:], bias.to_broadcast([P, 1])).then_inc(weights_loaded, 16)
            sp.wait_ge(total_step, 4)
            sp.dma_start(out, total[:]).then_inc(out_written, 16)
            sp.wait_ge(out_written, 16)

        @block.gpsimd
        def _(pool):
            with pool.Fori(0, PAIRS) as u:
                for s in range(2):
                    pool.wait_ge(index_ready, 2 * u + s + 1)
                    pool.sem_inc(gathers_begun, 1)
                    for f in range(F):
                        pool.indirect_dma_start(
                            out=rows[s][:, f, :], out_offset=None, in_=table,
                            in_offset=bass.IndirectOffsetOnAxis(ap=fslot[s][:, f:f + 1], axis=0),
                        ).then_inc(gathered[s], 16)
                    for w in range(L):
                        pool.indirect_dma_start(
                            out=words[s][:, w, :], out_offset=None, in_=title_table,
                            in_offset=bass.IndirectOffsetOnAxis(ap=tslot[s][:, w:w + 1], axis=0),
                        ).then_inc(gathered[s], 16)

        @block.vector
        def _(dve):
            def prepare(t, s):
                fi, ti = findex[:, t, :], tindex[:, t, :]
                if not isinstance(t, int) or t > 0:
                    dve.wait_ge(index_ready, t)
                nc.vector.tensor_scalar(fneg[:], fi, 0, V, ALU.is_lt, ALU.mult)
                nc.vector.tensor_scalar(tneg[:], ti, 0, VT, ALU.is_lt, ALU.mult).then_inc(index_step, 1)
                dve.wait_ge(index_step, 3 * t + 1)
                nc.vector.tensor_tensor(fslot[s][:], fneg[:], fi, ALU.add)
                nc.vector.tensor_tensor(tslot[s][:], tneg[:], ti, ALU.add).then_inc(index_step, 1)
                dve.wait_ge(index_step, 3 * t + 2)
                nc.vector.tensor_scalar(fneg[:], fslot[s][:], 0, V - 1, ALU.max, ALU.min)
                nc.vector.tensor_scalar(tslot[s][:], tslot[s][:], 0, VT - 1, ALU.max, ALU.min).then_inc(index_step, 1)
                dve.wait_ge(index_step, 3 * t + 3)
                nc.vector.tensor_tensor(fslot[s][:], fneg[:], fbase[:], ALU.add).then_inc(index_ready, 1)

            def tile(u, s, last):
                t = 2 * u + s
                dve.wait_ge(gathered[s], (F + L) * 16 * u + (F + L) * 16)
                dve.wait_ge(squared, t + 1)
                nc.vector.tensor_tensor(scaled[s][:, 0:F, :], rows[s][:, :, 0:E],
                                        fvalue[:, t, :].unsqueeze(2).to_broadcast([P, F, E]), ALU.mult)
                nc.vector.tensor_tensor(weighted[:], rows[s][:, :, E], fvalue[:, t, :], ALU.mult)
                nc.vector.tensor_tensor(wscaled[:], words[s][:],
                                        tvalue[:, t, :].unsqueeze(2).to_broadcast([P, L, E]),
                                        ALU.mult).then_inc(wscaled_ready, 1)
                dve.wait_ge(wscaled_ready, t + 1)
                if not last:
                    prepare(t + 2, s)
                nc.vector.tensor_reduce(fieldsum[s][:], scaled[s][:, 0:F, :].rearrange("p f e -> p e f"),
                                        AXX, ALU.add)
                nc.vector.tensor_reduce(first[:, bass.ds(t, 1)], weighted[:], AXX, ALU.add)
                nc.vector.tensor_reduce(scaled[s][:, F, :], wscaled[:].rearrange("p l e -> p e l"),
                                        AXX, ALU.add).then_inc(sums_ready, 1)
                dve.wait_ge(sums_ready, t + 1)

            nc.vector.memset(ones[:], 1.0).then_inc(ones_ready, 1)
            dve.wait_ge(index_loaded, 48)
            prepare(0, 0)
            prepare(1, 1)
            dve.wait_ge(values_loaded, 32)
            with dve.Fori(0, PAIRS - 1) as u:
                for s in range(2):
                    tile(u, s, last=False)
            for s in range(2):
                tile(PAIRS - 1, s, last=True)
            dve.wait_ge(squared, TILES + 2)
            dve.wait_ge(deep_ready, TILES)
            dve.wait_ge(weights_loaded, 6 * 16)
            nc.vector.tensor_tensor(diff[:], sq_of_sum[:], sum_of_sq[:], ALU.subtract)
            nc.vector.tensor_tensor(linear[:], first[:], deep[:], ALU.add).then_inc(total_step, 1)
            dve.wait_ge(total_step, 1)
            nc.vector.tensor_scalar(diff[:], diff[:], 0.5, None, ALU.mult).then_inc(total_step, 1)
            dve.wait_ge(total_step, 2)
            nc.vector.tensor_tensor(linear[:], linear[:], diff[:], ALU.add).then_inc(total_step, 1)
            dve.wait_ge(total_step, 3)
            nc.vector.tensor_scalar(total[:], linear[:], bias_sb[:], None, ALU.add).then_inc(total_step, 1)

        @block.tensor
        def _(pe):
            pe.wait_ge(video_loaded, 48)
            for c in range(B // VCHUNK):
                if c > 0:
                    pe.wait_ge(video_ready, c)
                nc.tensor.matmul(pv[LAST:P, :], vwt_sb[:], video_sb[:, c * VCHUNK:(c + 1) * VCHUNK],
                                 start=True, stop=True).then_inc(video_summed, 1)
            pe.wait_ge(weights_loaded, 6 * 16)
            pe.wait_ge(ones_ready, 1)
            with pe.Fori(0, PAIRS) as u:
                for s in range(2):
                    t = 2 * u + s
                    pe.wait_ge(sums_ready, t + 1)
                    for k in range(KB):
                        n = min(FPB, F + 1 - FPB * k)
                        last = nc.tensor.transpose(pt[k // FPB][0:n * E, k % FPB, :],
                                                   scaled[s][:, FPB * k:FPB * k + n, :].rearrange("p f e -> p (f e)"), ident[:])
                        if k in (FPB - 1, KB - 1):
                            last.then_inc(transposed, 1)
                    pe.wait_ge(xt_ready, 2 * t + 2)
                    for m in range(KH):
                        for k in range(KB):
                            last = nc.tensor.matmul(ph1[:, m, :], w1_sb[:, k, m * P:(m + 1) * P], xt[s][:, k, :],
                                                    start=(k == 0), stop=(k == KB - 1))
                    last.then_inc(h1_summed, 1)
                    pe.wait_ge(h1_ready, KH * (t + 1))
                    for m in range(K2):
                        for k in range(KH):
                            last = nc.tensor.matmul(ph2[:, m, :], w2_sb[:, k, m * P:(m + 1) * P], h1[s][:, k, :],
                                                    start=(k == 0), stop=(k == KH - 1))
                    last.then_inc(h2_summed, 1)
                    pe.wait_ge(h2_ready, K2 * (t + 1))
                    for m in range(K2):
                        last = nc.tensor.matmul(py[:, 0:1], h2[s][:, m, :], ones[:],
                                                start=(m == 0), stop=(m == K2 - 1))
                    last.then_inc(y_summed, 1)

        @block.scalar
        def _(act):
            act.sem_inc(squared, 2)
            act.wait_ge(video_loaded, 48)
            for c in range(B // VCHUNK):
                act.wait_ge(video_summed, c + 1)
                nc.scalar.activation(video_emb[LAST:P, c * VCHUNK:(c + 1) * VCHUNK], pv[LAST:P, :], ACT.Identity,
                                     bias=vb_sb[LAST:P, :]).then_inc(video_ready, 1)
            act.wait_ge(video_ready, B // VCHUNK)
            act.wait_ge(weights_loaded, 6 * 16)
            with act.Fori(0, PAIRS) as u:
                for s in range(2):
                    t = 2 * u + s
                    act.wait_ge(transposed, 2 * t + 1)
                    nc.scalar.activation(xt[s][:, 0:FPB, :], pt[0][:], ACT.Copy).then_inc(xt_ready, 1)
                    act.wait_ge(transposed, 2 * t + 2)
                    nc.scalar.activation(xt[s][LAST:P, KB - 1, :], video_emb[LAST:P, bass.ds(t * P, P)], ACT.Copy)
                    nc.scalar.activation(xt[s][0:LAST, KB - 1, :], pt[1][0:LAST, KB - 1 - FPB, :], ACT.Copy)
                    nc.scalar.activation(xt[s][:, FPB:KB - 1, :], pt[1][:, 0:KB - 1 - FPB, :],
                                         ACT.Copy).then_inc(xt_ready, 1)
                    act.wait_ge(sums_ready, t + 1)
                    nc.scalar.activation(square[:], scaled[s][:, 0:F, :], ACT.Square,
                                         accum_out=sum_of_sq[:, bass.ds(t, 1)])
                    nc.scalar.activation(square_s[:], fieldsum[s][:], ACT.Square,
                                         accum_out=sq_of_sum[:, bass.ds(t, 1)]).then_inc(squared, 1)
                    act.wait_ge(h1_summed, t + 1)
                    for m in range(KH):
                        nc.scalar.activation(h1[s][:, m, :], ph1[:, m, :], ACT.Relu,
                                             bias=b1_sb[:, m:m + 1]).then_inc(h1_ready, 1)
                    act.wait_ge(h2_summed, t + 1)
                    for m in range(K2):
                        nc.scalar.activation(h2[s][:, m, :], ph2[:, m, :], ACT.Relu,
                                             bias=b2_sb[:, m:m + 1]).then_inc(h2_ready, 1)
                    act.wait_ge(y_summed, t + 1)
                    nc.scalar.activation(deep[:, bass.ds(t, 1)], py[:, 0:1], ACT.Copy).then_inc(deep_ready, 1)


def kernel(r_Xi, r_title_feature, L0_rec_Xv, L0_rec_video_feature, L0_rec_title_value, L0_rec_first_tables,
           L0_rec_second_tables, L0_rec_title_table, L0_rec_video_W, L0_rec_video_b, L0_rec_W1, L0_rec_b1,
           L0_rec_W2, L0_rec_b2, L0_rec_bias):
    import numpy as np
    import concourse.bacc as bacc
    from concourse.bass_utils import run_bass_kernel_spmd

    def tiles(a):
        return np.ascontiguousarray(np.asarray(a).reshape(TILES, P, -1).transpose(1, 0, 2))

    c = np.ascontiguousarray
    table = np.concatenate([np.asarray(L0_rec_second_tables), np.asarray(L0_rec_first_tables)[:, :, None]], axis=2)
    arrays = {
        "table": table.reshape(F * V, EA),
        "title_table": c(L0_rec_title_table),
        "field_index": tiles(np.asarray(r_Xi)[:, :, 0]),
        "field_value": tiles(L0_rec_Xv),
        "title_index": tiles(r_title_feature),
        "title_value": tiles(L0_rec_title_value),
        "video_t": c(np.asarray(L0_rec_video_feature).T),
        "video_wt": c(np.asarray(L0_rec_video_W).T),
        "video_b": c(np.asarray(L0_rec_video_b).reshape(E, 1)),
        "w1": c(L0_rec_W1),
        "b1": c(np.asarray(L0_rec_b1).reshape(KH, P).T),
        "w2": c(L0_rec_W2),
        "b2": c(np.asarray(L0_rec_b2).reshape(K2, P).T),
        "bias": c(np.asarray(L0_rec_bias).reshape(1, 1)),
        "field_base": c(np.broadcast_to(np.arange(F, dtype=np.int32) * V, (P, F))),
        "identity": np.eye(P, dtype=np.float32),
    }
    nc = bacc.Bacc("TRN2", target_bir_lowering=False, num_devices=1)
    args = [nc.dram_tensor(f"in_{k}", a.shape, mybir.dt.from_np(a.dtype), kind="ExternalInput").ap()
            for k, a in arrays.items()]
    out = nc.dram_tensor("out", (P, TILES), mybir.dt.float32, kind="ExternalOutput").ap()
    build(nc, *args, out)
    r = run_bass_kernel_spmd(nc, [{f"in_{k}": a for k, a in arrays.items()}], core_ids=[0])
    return np.asarray(r.results[0]["out"]).T.reshape(B)
```

```python
from contextlib import ExitStack

import concourse.bass as bass
from concourse import mybir

B = 2048
F = 26
V = 12500
E = 32
EA = E + 1
VT = 6250
L = 20
DVF = 128
H1, H2 = 512, 256
P = 128
TILES = B // P
PAIRS = TILES // 2
FPB = P // E
KF = -(-F // FPB)
FREST = F * E - (KF - 1) * P
KREST = FREST + E
KB = KF + 1
KH = H1 // P
K2 = H2 // P
VCHUNK = 512
BANK = 512

HI = -(-VT // P)
GI = P // L
Q = GI * L
GROUPS = -(-P // GI)
GP = GROUPS // 2
W = HI * GI
BANKS = 4
SPLITS = 3


def build(nc, table, title_table, field_index, field_value, title_index, title_value, video_t, video_wt,
          video_b, w1, b1, w2, b2, bias, field_base, item_of_word, counting_row, identity, out):
    fp32, bf16, i32, i16 = mybir.dt.float32, mybir.dt.bfloat16, mybir.dt.int32, mybir.dt.int16
    ALU = mybir.AluOpType
    ACT = mybir.ActivationFunctionType
    AXX = mybir.AxisListType.X
    ctx = ExitStack()
    with ctx:
        def sb(name, shape, dt=fp32):
            return ctx.enter_context(nc.sbuf_tensor(name, shape, dt))

        def ps(name, shape):
            return ctx.enter_context(nc.psum_tensor(name, shape, fp32))

        def sem(name):
            return ctx.enter_context(nc.semaphore(name))

        findex = sb("findex", [P, TILES, F], i32)
        fvalue = sb("fvalue", [P, TILES, F])
        fbase = sb("fbase", [P, F], i32)
        fneg = sb("fneg", [P, F])
        fslot = [sb(f"fslot{s}", [P, F], i32) for s in range(2)]
        rows = [sb(f"rows{s}", [P, F, EA]) for s in range(2)]
        scaled = [sb(f"scaled{s}", [P, F * E]) for s in range(2)]
        fieldsum = [sb(f"fieldsum{s}", [P, E]) for s in range(2)]
        weighted = sb("weighted", [P, F])
        square = sb("square", [P, F * E])
        square_s = sb("square_s", [P, E])

        tindex = sb("tindex", [Q, TILES, GROUPS], i32)
        twrap = sb("twrap", [Q, TILES, GROUPS], i32)
        thi = sb("thi", [Q, TILES, GROUPS], i32)
        tvalue = sb("tvalue", [Q, TILES, GROUPS])
        trest = sb("trest", [Q, TILES, GROUPS])
        tpart = sb("tpart", [Q, TILES, GROUPS], bf16)
        item = sb("item", [Q, 1])
        counting = sb("counting", [Q, W], i16)
        word = sb("word", [Q, TILES, 2 + SPLITS, GROUPS])
        wslot = sb("wslot", [Q, 2 + SPLITS, GROUPS])
        lo_hot = [sb(f"lo_hot{i}", [Q, P], bf16) for i in range(BANKS)]
        hi_hot = [sb(f"hi_hot{i}", [Q, SPLITS, W], bf16) for i in range(BANKS)]
        weight = sb("weight", [P, GROUPS, W])
        ttable = sb("ttable", [P, HI, E])

        ident = sb("ident", [P, P])
        video_sb = sb("video_sb", [P, B])
        vwt_sb = sb("vwt_sb", [P, E])
        vb_sb = sb("vb_sb", [P, 1])
        video_emb = sb("video_emb", [P, B])
        w1_sb = sb("w1_sb", [P, KB, H1])
        w2_sb = sb("w2_sb", [P, KH, H2])
        b1_sb = sb("b1_sb", [P, KH])
        b2_sb = sb("b2_sb", [P, K2])
        bias_sb = sb("bias_sb", [P, 1])
        ones = sb("ones", [P, 1])
        xt = [sb(f"xt{s}", [P, KB, P]) for s in range(2)]
        h1 = [sb(f"h1{s}", [P, KH, P]) for s in range(2)]
        h2 = [sb(f"h2{s}", [P, K2, P]) for s in range(2)]
        sq_of_sum = sb("sq_of_sum", [P, TILES])
        sum_of_sq = sb("sum_of_sq", [P, TILES])
        first = sb("first", [P, TILES])
        deep = sb("deep", [P, TILES])
        diff = sb("diff", [P, TILES])
        linear = sb("linear", [P, TILES])
        total = sb("total", [P, TILES])

        pw = ps("pw", [P, BANKS, BANK])
        pt = [ps("pt0", [P, FPB, P]), ps("pt1", [P, FPB, P])]
        ph1 = ps("ph1", [P, KH, P])
        pc = ps("pc", [P, BANK])
        ph2 = pc[:, 0:H2].rearrange("p (m n) -> p m n", n=P)
        py = pc[:, H2:H2 + 1]
        ptitle = pc[:, H2 + 2:H2 + 2 + GROUPS * GI]

        index_loaded = sem("index_loaded")
        words_loaded = sem("words_loaded")
        values_loaded = sem("values_loaded")
        weights_loaded = sem("weights_loaded")
        title_loaded = sem("title_loaded")
        video_loaded = sem("video_loaded")
        index_step = sem("index_step")
        index_ready = sem("index_ready")
        word_step = sem("word_step")
        wslot_ready = sem("wslot_ready")
        hots_ready = sem("hots_ready")
        hots_used = sem("hots_used")
        weight_copied = sem("weight_copied")
        title_summed = sem("title_summed")
        title_ready = sem("title_ready")
        gathers_begun = sem("gathers_begun")
        gathered = [sem(f"gathered{s}") for s in range(2)]
        scaled_ready = sem("scaled_ready")
        sums_ready = sem("sums_ready")
        squared = sem("squared")
        transposed = sem("transposed")
        ones_ready = sem("ones_ready")
        xt_ready = sem("xt_ready")
        h1_summed = sem("h1_summed")
        h1_ready = sem("h1_ready")
        h2_summed = sem("h2_summed")
        h2_ready = sem("h2_ready")
        y_summed = sem("y_summed")
        deep_ready = sem("deep_ready")
        video_summed = sem("video_summed")
        video_ready = sem("video_ready")
        total_step = sem("total_step")
        out_written = sem("out_written")
        block = ctx.enter_context(nc.Block())

        @block.sync
        def _(sp):
            sp.dma_start(findex[:], field_index).then_inc(index_loaded, 16)
            sp.dma_start(fbase[:], field_base).then_inc(index_loaded, 16)
            sp.dma_start(tindex[:], title_index).then_inc(words_loaded, 16)
            sp.dma_start(tvalue[:], title_value).then_inc(words_loaded, 16)
            sp.dma_start(item[:], item_of_word).then_inc(words_loaded, 16)
            sp.dma_start(counting[:], counting_row).then_inc(words_loaded, 16)
            sp.dma_start(fvalue[:], field_value).then_inc(values_loaded, 16)
            sp.dma_start(ttable[:], title_table).then_inc(title_loaded, 16)
            sp.dma_start(video_sb[:], video_t).then_inc(video_loaded, 16)
            sp.dma_start(vwt_sb[:], video_wt).then_inc(video_loaded, 16)
            sp.dma_start(vb_sb[FREST:KREST, :], video_b).then_inc(video_loaded, 16)
            sp.dma_start(ident[:], identity).then_inc(weights_loaded, 16)
            sp.dma_start(w1_sb[:, 0:KF - 1, :],
                         w1[0:(KF - 1) * P, :].rearrange("(k p) n -> p k n", p=P)).then_inc(weights_loaded, 16)
            sp.dma_start(w1_sb[0:FREST, KF - 1, :], w1[(KF - 1) * P:F * E, :]).then_inc(weights_loaded, 16)
            sp.dma_start(w1_sb[FREST:KREST, KF - 1, :], w1[(F + 1) * E:(F + 2) * E, :]).then_inc(weights_loaded, 16)
            for g in range(FPB):
                sp.dma_start(w1_sb[g * E:(g + 1) * E, KF, :], w1[F * E:(F + 1) * E, :]).then_inc(weights_loaded, 16)
            sp.dma_start(w2_sb[:], w2.rearrange("(k p) n -> p k n", p=P)).then_inc(weights_loaded, 16)
            sp.dma_start(b1_sb[:], b1).then_inc(weights_loaded, 16)
            sp.dma_start(b2_sb[:], b2).then_inc(weights_loaded, 16)
            sp.dma_start(bias_sb[:], bias.to_broadcast([P, 1])).then_inc(weights_loaded, 16)
            sp.wait_ge(total_step, 4)
            sp.dma_start(out, total[:]).then_inc(out_written, 16)
            sp.wait_ge(out_written, 16)

        WEIGHTS = (8 + FPB) * 16

        @block.gpsimd
        def _(pool):
            with pool.Fori(0, PAIRS) as u:
                for s in range(2):
                    pool.wait_ge(index_ready, 2 * u + s + 1)
                    pool.sem_inc(gathers_begun, 1)
                    for f in range(F):
                        pool.indirect_dma_start(
                            out=rows[s][:, f, :], out_offset=None, in_=table,
                            in_offset=bass.IndirectOffsetOnAxis(ap=fslot[s][:, f:f + 1], axis=0),
                        ).then_inc(gathered[s], 16)

        @block.vector
        def _(dve):
            def prepare(t, s):
                fi = findex[:, t, :]
                if not isinstance(t, int) or t > 0:
                    dve.wait_ge(index_ready, t)
                nc.vector.tensor_scalar(fneg[:], fi, 0, V, ALU.is_lt, ALU.mult).then_inc(index_step, 1)
                dve.wait_ge(index_step, 3 * t + 1)
                nc.vector.tensor_tensor(fslot[s][:], fneg[:], fi, ALU.add).then_inc(index_step, 1)
                dve.wait_ge(index_step, 3 * t + 2)
                nc.vector.tensor_scalar(fneg[:], fslot[s][:], 0, V - 1, ALU.max, ALU.min).then_inc(index_step, 1)
                dve.wait_ge(index_step, 3 * t + 3)
                nc.vector.tensor_tensor(fslot[s][:], fneg[:], fbase[:], ALU.add).then_inc(index_ready, 1)

            def split_words():
                done = [0]

                def link(ins):
                    done[0] += 1
                    ins.then_inc(word_step, 1)
                    dve.wait_ge(word_step, done[0])

                link(nc.vector.tensor_scalar(trest[:], tindex[:], 0, VT, ALU.is_lt, ALU.mult))
                link(nc.vector.tensor_tensor(trest[:], trest[:], tindex[:], ALU.add))
                link(nc.vector.tensor_scalar(twrap[:], trest[:], 0, VT - 1, ALU.max, ALU.min))
                link(nc.vector.tensor_scalar(thi[:], twrap[:], 7, None, ALU.arith_shift_right))
                link(nc.vector.tensor_scalar(word[:, :, 1, :], thi[:], GI, item[:], ALU.mult, ALU.add))
                link(nc.vector.tensor_scalar(thi[:], twrap[:], P - 1, None, ALU.bitwise_and))
                link(nc.vector.tensor_copy(word[:, :, 0, :], thi[:]))
                rest = tvalue
                for k in range(SPLITS):
                    link(nc.vector.tensor_copy(tpart[:], rest[:]))
                    link(nc.vector.tensor_copy(word[:, :, 2 + k, :], tpart[:]))
                    if k < SPLITS - 1:
                        link(nc.vector.tensor_tensor(trest[:], rest[:], tpart[:], ALU.subtract))
                    rest = trest

            def one_hots(t, odd):
                if not isinstance(t, int) or t > 0:
                    dve.wait_ge(hots_ready, t * GROUPS)
                nc.vector.tensor_copy(wslot[:], word[:, t, :, :]).then_inc(wslot_ready, 1)
                dve.wait_ge(wslot_ready, t + 1)
                for g in range(GROUPS):
                    i = (odd * GROUPS + g) % BANKS
                    dve.wait_ge(hots_used, t * GROUPS + g + 1)
                    nc.vector.tensor_scalar(lo_hot[i][:], counting[:, 0:P], wslot[:, 0, g:g + 1], None, ALU.is_equal)
                    for k in range(SPLITS):
                        last = nc.vector.tensor_scalar(hi_hot[i][:, k, :], counting[:], wslot[:, 1, g:g + 1],
                                                       wslot[:, 2 + k, g:g + 1], ALU.is_equal, ALU.mult)
                    last.then_inc(hots_ready, 1)

            def fields(u, s, prepared):
                t = 2 * u + s
                dve.wait_ge(gathered[s], F * 16 * u + F * 16)
                dve.wait_ge(squared, t + 1)
                nc.vector.tensor_tensor(scaled[s][:].rearrange("p (f e) -> p f e", e=E), rows[s][:, :, 0:E],
                                        fvalue[:, t, :].unsqueeze(2).to_broadcast([P, F, E]), ALU.mult)
                nc.vector.tensor_tensor(weighted[:], rows[s][:, :, E], fvalue[:, t, :],
                                        ALU.mult).then_inc(scaled_ready, 1)
                dve.wait_ge(scaled_ready, t + 1)
                if prepared:
                    prepare(t + 2, s)
                nc.vector.tensor_reduce(first[:, bass.ds(t, 1)], weighted[:], AXX, ALU.add)
                nc.vector.tensor_reduce(fieldsum[s][:], scaled[s][:].rearrange("p (f e) -> p e f", e=E),
                                        AXX, ALU.add).then_inc(sums_ready, 1)
                dve.wait_ge(sums_ready, t + 1)

            nc.vector.memset(ones[:], 1.0).then_inc(ones_ready, 1)
            dve.wait_ge(index_loaded, 32)
            prepare(0, 0)
            prepare(1, 1)
            dve.wait_ge(words_loaded, 64)
            split_words()
            dve.wait_ge(values_loaded, 16)
            one_hots(0, 0)
            with dve.Fori(0, PAIRS - 1) as u:
                for s in range(2):
                    fields(u, s, prepared=True)
                    one_hots(2 * u + s + 1, 1 - s)
            fields(PAIRS - 1, 0, prepared=False)
            one_hots(TILES - 1, 1)
            fields(PAIRS - 1, 1, prepared=False)
            dve.wait_ge(squared, TILES + 2)
            dve.wait_ge(weights_loaded, WEIGHTS)
            nc.vector.tensor_tensor(diff[:], sq_of_sum[:], sum_of_sq[:], ALU.subtract).then_inc(total_step, 1)
            dve.wait_ge(total_step, 1)
            nc.vector.tensor_scalar(diff[:], diff[:], 0.5, None, ALU.mult).then_inc(total_step, 1)
            dve.wait_ge(total_step, 2)
            nc.vector.scalar_tensor_tensor(linear[:], first[:], bias_sb[:], diff[:], ALU.add,
                                           ALU.add).then_inc(total_step, 1)
            dve.wait_ge(total_step, 3)
            dve.wait_ge(deep_ready, TILES)
            nc.vector.tensor_tensor(total[:], linear[:], deep[:], ALU.add).then_inc(total_step, 1)

        STAGES = [range(0, 2), range(2, 4), range(4, 6), range(6, GP)]

        @block.tensor
        def _(pe):
            def products(t, odd, pairs):
                for j in pairs:
                    for g in (2 * j, 2 * j + 1):
                        i = (odd * GROUPS + g) % BANKS
                        pe.wait_ge(hots_ready, t * GROUPS + g + 1)
                        if g % 2 == 0:
                            pe.wait_ge(weight_copied, t * GP + j + 1)
                        for k in range(SPLITS):
                            last = nc.tensor.matmul(pw[:, i, 0:W], lo_hot[i][:], hi_hot[i][:, k, :],
                                                    start=(k == 0), stop=(k == SPLITS - 1))
                        last.then_inc(hots_used, 1)

            def title(t):
                pe.wait_ge(weight_copied, t * GP + GP + BANKS // 2)
                if not isinstance(t, int) or t > 0:
                    pe.wait_ge(deep_ready, t)
                for h in range(HI):
                    g = h % FPB
                    last = nc.tensor.matmul(ptitle[g * E:(g + 1) * E, :], ttable[:, h, :],
                                            weight[:, :, h * GI:(h + 1) * GI], start=(h < FPB), stop=(h >= HI - FPB))
                last.then_inc(title_summed, 1)

            def tile(u, s, more):
                t = 2 * u + s
                pe.wait_ge(scaled_ready, t + 1)
                for k in range(KF):
                    n = min(P, F * E - P * k)
                    last = nc.tensor.transpose(pt[k // FPB][0:n, k % FPB, :], scaled[s][:, P * k:P * k + n], ident[:])
                    if k in (FPB - 1, KF - 1):
                        last.then_inc(transposed, 1)
                if more:
                    products(t + 1, 1 - s, STAGES[0])
                pe.wait_ge(xt_ready, 2 * t + 2)
                pe.wait_ge(title_ready, t + 1)
                for m in range(KH):
                    for k in range(KB):
                        n = KREST if k == KF - 1 else P
                        last = nc.tensor.matmul(ph1[:, m, :], w1_sb[0:n, k, m * P:(m + 1) * P], xt[s][0:n, k, :],
                                                start=(k == 0), stop=(k == KB - 1))
                last.then_inc(h1_summed, 1)
                if more:
                    products(t + 1, 1 - s, STAGES[1])
                pe.wait_ge(h1_ready, t + 1)
                for m in range(K2):
                    for k in range(KH):
                        last = nc.tensor.matmul(ph2[:, m, :], w2_sb[:, k, m * P:(m + 1) * P], h1[s][:, k, :],
                                                start=(k == 0), stop=(k == KH - 1))
                last.then_inc(h2_summed, 1)
                if more:
                    products(t + 1, 1 - s, STAGES[2])
                pe.wait_ge(h2_ready, t + 1)
                for m in range(K2):
                    last = nc.tensor.matmul(py, h2[s][:, m, :], ones[:], start=(m == 0), stop=(m == K2 - 1))
                last.then_inc(y_summed, 1)
                if more:
                    products(t + 1, 1 - s, STAGES[3])
                    title(t + 1)

            pe.wait_ge(video_loaded, 48)
            for c in range(B // VCHUNK):
                nc.tensor.matmul(pw[FREST:KREST, c, :], vwt_sb[:], video_sb[:, c * VCHUNK:(c + 1) * VCHUNK],
                                 start=True, stop=True).then_inc(video_summed, 1)
            pe.wait_ge(title_loaded, 16)
            pe.wait_ge(video_ready, B // VCHUNK)
            products(0, 0, range(GP))
            title(0)
            pe.wait_ge(weights_loaded, WEIGHTS)
            pe.wait_ge(ones_ready, 1)
            with pe.Fori(0, PAIRS - 1) as u:
                for s in range(2):
                    tile(u, s, more=True)
            tile(PAIRS - 1, 0, more=True)
            tile(PAIRS - 1, 1, more=False)

        @block.scalar
        def _(act):
            def weights(t, odd, pairs):
                for j in pairs:
                    i = (odd * GROUPS + 2 * j) % BANKS
                    act.wait_ge(hots_used, t * GROUPS + 2 * j + 2 + BANKS)
                    nc.scalar.activation(weight[:, 2 * j:2 * j + 2, :], pw[:, i:i + 2, 0:W],
                                         ACT.Copy).then_inc(weight_copied, 1)

            def title(t, s):
                act.wait_ge(title_summed, t + 1)
                nc.scalar.activation(xt[s][:, KF, :], ptitle[:, 0:P], ACT.Copy).then_inc(title_ready, 1)

            def tile(u, s, more):
                t = 2 * u + s
                act.wait_ge(transposed, 2 * t + 1)
                nc.scalar.activation(xt[s][:, 0:FPB, :], pt[0][:], ACT.Copy).then_inc(xt_ready, 1)
                act.wait_ge(transposed, 2 * t + 2)
                nc.scalar.activation(xt[s][FREST:KREST, KF - 1, :], video_emb[FREST:KREST, bass.ds(t * P, P)], ACT.Copy)
                nc.scalar.activation(xt[s][0:FREST, KF - 1, :], pt[1][0:FREST, KF - 1 - FPB, :], ACT.Copy)
                nc.scalar.activation(xt[s][:, FPB:KF - 1, :], pt[1][:, 0:KF - 1 - FPB, :],
                                     ACT.Copy).then_inc(xt_ready, 1)
                if more:
                    weights(t + 1, 1 - s, STAGES[0])
                act.wait_ge(sums_ready, t + 1)
                nc.scalar.activation(square[:], scaled[s][:], ACT.Square, accum_out=sum_of_sq[:, bass.ds(t, 1)])
                nc.scalar.activation(square_s[:], fieldsum[s][:], ACT.Square,
                                     accum_out=sq_of_sum[:, bass.ds(t, 1)]).then_inc(squared, 1)
                act.wait_ge(h1_summed, t + 1)
                for m in range(KH):
                    last = nc.scalar.activation(h1[s][:, m, :], ph1[:, m, :], ACT.Relu, bias=b1_sb[:, m:m + 1])
                last.then_inc(h1_ready, 1)
                if more:
                    weights(t + 1, 1 - s, STAGES[1])
                act.wait_ge(h2_summed, t + 1)
                for m in range(K2):
                    last = nc.scalar.activation(h2[s][:, m, :], ph2[:, m, :], ACT.Relu, bias=b2_sb[:, m:m + 1])
                last.then_inc(h2_ready, 1)
                if more:
                    weights(t + 1, 1 - s, STAGES[2])
                act.wait_ge(y_summed, t + 1)
                nc.scalar.activation(deep[:, bass.ds(t, 1)], py, ACT.Copy).then_inc(deep_ready, 1)
                if more:
                    weights(t + 1, 1 - s, STAGES[3])
                    title(t + 1, 1 - s)

            act.sem_inc(squared, 2)
            act.sem_inc(hots_used, BANKS)
            act.sem_inc(weight_copied, BANKS // 2)
            act.wait_ge(video_loaded, 48)
            for c in range(B // VCHUNK):
                act.wait_ge(video_summed, c + 1)
                nc.scalar.activation(video_emb[FREST:KREST, c * VCHUNK:(c + 1) * VCHUNK], pw[FREST:KREST, c, :],
                                     ACT.Identity, bias=vb_sb[FREST:KREST, :]).then_inc(video_ready, 1)
            act.wait_ge(video_ready, B // VCHUNK)
            weights(0, 0, range(GP))
            title(0, 0)
            act.wait_ge(weights_loaded, WEIGHTS)
            with act.Fori(0, PAIRS - 1) as u:
                for s in range(2):
                    tile(u, s, more=True)
            tile(PAIRS - 1, 0, more=True)
            tile(PAIRS - 1, 1, more=False)

def kernel(r_Xi, r_title_feature, L0_rec_Xv, L0_rec_video_feature, L0_rec_title_value, L0_rec_first_tables,
           L0_rec_second_tables, L0_rec_title_table, L0_rec_video_W, L0_rec_video_b, L0_rec_W1, L0_rec_b1,
           L0_rec_W2, L0_rec_b2, L0_rec_bias):
    import numpy as np
    import concourse.bacc as bacc
    from concourse.bass_utils import run_bass_kernel_spmd

    def tiles(a):
        return np.ascontiguousarray(np.asarray(a).reshape(TILES, P, -1).transpose(1, 0, 2))

    def word_groups(a):
        a = np.asarray(a)
        padded = np.zeros((TILES, GROUPS * GI, L), a.dtype)
        padded[:, :P] = a.reshape(TILES, P, L)
        return np.ascontiguousarray(padded.reshape(TILES, GROUPS, Q).transpose(2, 0, 1))

    c = np.ascontiguousarray
    table = np.concatenate([np.asarray(L0_rec_second_tables), np.asarray(L0_rec_first_tables)[:, :, None]], axis=2)
    title = np.zeros((HI * P, E), np.float32)
    title[:VT] = np.asarray(L0_rec_title_table)
    w1 = np.asarray(L0_rec_W1)
    arrays = {
        "table": table.reshape(F * V, EA),
        "title_table": c(title.reshape(HI, P, E).transpose(1, 0, 2)),
        "field_index": tiles(np.asarray(r_Xi)[:, :, 0]),
        "field_value": tiles(L0_rec_Xv),
        "title_index": word_groups(r_title_feature),
        "title_value": word_groups(L0_rec_title_value),
        "video_t": c(np.asarray(L0_rec_video_feature).T),
        "video_wt": c(np.asarray(L0_rec_video_W).T),
        "video_b": c(np.asarray(L0_rec_video_b).reshape(E, 1)),
        "w1": c(w1),
        "b1": c(np.asarray(L0_rec_b1).reshape(KH, P).T),
        "w2": c(L0_rec_W2),
        "b2": c(np.asarray(L0_rec_b2).reshape(K2, P).T),
        "bias": c(np.asarray(L0_rec_bias).reshape(1, 1)),
        "field_base": c(np.broadcast_to(np.arange(F, dtype=np.int32) * V, (P, F))),
        "item_of_word": (np.arange(Q, dtype=np.float32) // L).reshape(Q, 1),
        "counting": c(np.broadcast_to(np.arange(W, dtype=np.int16), (Q, W))),
        "identity": np.eye(P, dtype=np.float32),
    }
    nc = bacc.Bacc("TRN2", target_bir_lowering=False, num_devices=1)
    args = [nc.dram_tensor(f"in_{k}", a.shape, mybir.dt.from_np(a.dtype), kind="ExternalInput").ap()
            for k, a in arrays.items()]
    out = nc.dram_tensor("out", (P, TILES), mybir.dt.float32, kind="ExternalOutput").ap()
    build(nc, *args, out)
    r = run_bass_kernel_spmd(nc, [{f"in_{k}": a for k, a in arrays.items()}], core_ids=[0])
    return np.asarray(r.results[0]["out"]).T.reshape(B)
```

```python
from contextlib import ExitStack

import concourse.bass as bass
from concourse import mybir

B = 2048
F = 26
V = 12500
E = 32
EA = E + 1
VT = 6250
L = 20
H1, H2 = 512, 256
P = 128
TILES = B // P
PAIRS = TILES // 2
FPB = P // E
KB = -(-F // FPB)
FREST = F * E - (KB - 1) * P
VIDEO = slice(FREST, FREST + E)
TITLE = slice(FREST + E, P)
KH = H1 // P
K2 = H2 // P
OWN = 2
G = F - OWN
SHARES = [(0, FPB), (KB - 1, KB)] + [(k, k + 1) for k in range(FPB, KB - 1)]
VCHUNK = 512
BANK = 512

HI = -(-VT // P)
LO_BITS = P.bit_length() - 1
PARTS = 3
GI = P // (L * PARTS)
Q = PARTS * GI * L
GROUPS = P // GI
W = GI * HI
BANKS = 4
GB = 4
GC = BANKS * GB
CHUNKS = GROUPS // GC

FIRST = 3
LAST_G = F - 1
CAND = 8
C_BITS = CAND.bit_length() - 1
VP = -(-V // CAND) * CAND
JS = -(-V // (CAND * P))
CW = CAND * EA
PJ = 5
PIECES = [(k, j, min(j + PJ, JS)) for k in range(OWN) for j in range(0, JS, PJ)]
SLOTS = 2
A_STAGES = [range(0, 7), range(7, JS)]

AHEAD = 2


def build(nc, table, own_table, own_index, title_table, field_index, field_value, title_index, title_value,
          video_t, video_wt, video_b, w1, b1, w2, b2, bias, field_base, word_constants, counting_row,
          q_constants, candidate_row, identity, fold, out):
    fp32, bf16, i32, i16 = mybir.dt.float32, mybir.dt.bfloat16, mybir.dt.int32, mybir.dt.int16
    ALU = mybir.AluOpType
    ACT = mybir.ActivationFunctionType
    AXX = mybir.AxisListType.X
    ctx = ExitStack()
    with ctx:
        def sb(name, shape, dt=fp32):
            return ctx.enter_context(nc.sbuf_tensor(name, shape, dt))

        def ps(name, shape):
            return ctx.enter_context(nc.psum_tensor(name, shape, fp32))

        def sem(name):
            return ctx.enter_context(nc.semaphore(name))

        findex = sb("findex", [P, TILES, F], i32)
        fvalue = sb("fvalue", [P, TILES, F])
        fbase = sb("fbase", [P, F], i32)
        fneg = sb("fneg", [P, F])
        fslot = [sb(f"fslot{s}", [P, F], i32) for s in range(2)]
        rows = [sb(f"rows{s}", [P, F, EA]) for s in range(2)]
        scaled = [sb(f"scaled{s}", [P, F * E]) for s in range(2)]
        fieldsum = [sb(f"fieldsum{s}", [P, E]) for s in range(2)]
        weighted = sb("weighted", [P, F])
        square = sb("square", [P, F * E])
        square_s = sb("square_s", [P, E])
        early_squares = sb("early_squares", [P, 1])

        tindex = sb("tindex", [Q, TILES, GROUPS], i32)
        tvalue = sb("tvalue", [Q, TILES, GROUPS])
        wconst = sb("wconst", [Q, PARTS])
        count16 = sb("count16", [Q, P], i16)
        counting = sb("counting", [Q, P], bf16)
        wneg = sb("wneg", [Q, GROUPS])
        wsum = sb("wsum", [Q, GROUPS])
        wrow = sb("wrow", [Q, GROUPS], i32)
        whi = sb("whi", [Q, GROUPS], i32)
        wlo = sb("wlo", [Q, GROUPS], i32)
        wpart = [sb(f"wpart{k}", [Q, GROUPS], bf16) for k in range(PARTS - 1)]
        wrest = [sb(f"wrest{k}", [Q, GROUPS]) for k in range(PARTS - 1)]
        lo2 = sb("lo2", [Q, GROUPS, 2], bf16)
        key2 = sb("key2", [Q, GROUPS, 2], bf16)
        part2 = sb("part2", [Q, GROUPS, 2], bf16)
        lo_hot = [sb(f"lo_hot{i}", [Q, GC, P], bf16) for i in range(CHUNKS)]
        hi_hot = [sb(f"hi_hot{i}", [Q, GC, W], bf16) for i in range(2)]
        hi_part = [sb(f"hi_part{i}", [Q, GC, W], bf16) for i in range(CHUNKS)]
        weight = sb("weight", [P, HI, P])
        ttable = sb("ttable", [P, HI, E])

        own_part = [[sb(f"own_part{k}_{part}", [P, JS, CW], bf16) for part in range(PARTS)] for k in range(OWN)]
        orow = [sb(f"orow{s}", [P, OWN, P], i32) for s in range(2)]
        oneg = sb("oneg", [P, OWN, P])
        osum = sb("osum", [P, OWN, P])
        oclamped = sb("oclamped", [P, OWN, P], i32)
        oq = sb("oq", [P, OWN, P], i32)
        q_row = sb("q_row", [P, OWN, P], i16)
        q_of = sb("q_of", [P, JS, 2], i16)
        q_hot = [sb(f"q_hot{k}", [P, JS, P], bf16) for k in range(OWN)]
        ocand = [sb(f"ocand{s}", [P, OWN], i32) for s in range(2)]
        cand_of = sb("cand_of", [P, CW])
        picked = sb("picked", [P, CW])

        ident = sb("ident", [P, P])
        video_sb = weight[:].rearrange("p h n -> p (h n)")[:, 0:B]
        vwt_sb = sb("vwt_sb", [P, E])
        vb_sb = sb("vb_sb", [P, 1])
        video_emb = sb("video_emb", [P, B])
        w1_sb = sb("w1_sb", [P, KB, H1])
        piece = [sb(f"piece{i}", [P, PJ, CW]) for i in range(SLOTS)]
        w2_sb = sb("w2_sb", [P, KH, H2])
        b1_sb = sb("b1_sb", [P, KH])
        b2_sb = sb("b2_sb", [P, K2])
        bias_sb = sb("bias_sb", [P, 1])
        ones = sb("ones", [P, 1])
        xt = [sb(f"xt{s}", [P, KB, P]) for s in range(2)]
        title_sums = sb("title_sums", [P, P])
        fold_sb = sb("fold_sb", [P, E])
        h1 = [sb(f"h1{s}", [P, KH, P]) for s in range(2)]
        h2 = [sb(f"h2{s}", [P, K2, P]) for s in range(2)]
        sq_of_sum = sb("sq_of_sum", [P, TILES])
        sum_of_sq = sb("sum_of_sq", [P, TILES])
        first = sb("first", [P, TILES])
        deep = sb("deep", [P, TILES])
        diff = sb("diff", [P, TILES])
        linear = sb("linear", [P, TILES])
        total = sb("total", [P, TILES])

        pw = ps("pw", [P, BANKS, BANK])
        pt = [ps("pt0", [P, FPB, P]), ps("pt1", [P, FPB, P])]
        ph1 = pt[0]
        ptitle = pt[1][:, FPB - 1, :]
        pf = ps("pf", [P, BANK])
        pcand = pf[:, 0:CW]
        pc = ps("pc", [P, BANK])
        ph2 = pc[:, 0:H2].rearrange("p (m n) -> p m n", n=P)
        py = pc[:, H2:H2 + 1]
        share_pt = [pt[0], pf[:].rearrange("p (m n) -> p m n", n=P), pt[1], pt[0]]
        last_ph1 = [pw[:, m, 0:P] for m in range(KH)]
        last_ph2 = [pt[1][:, 0, :], pf[:, 0:P]]

        first_index_loaded = sem("first_index_loaded")
        index_loaded = sem("index_loaded")
        words_loaded = sem("words_loaded")
        values_loaded = sem("values_loaded")
        weights_loaded = sem("weights_loaded")
        title_loaded = sem("title_loaded")
        video_loaded = sem("video_loaded")
        index_step = sem("index_step")
        index_ready = sem("index_ready")
        word_step = sem("word_step")
        counting_ready = sem("counting_ready")
        hi_hot_ready = sem("hi_hot_ready")
        hots_ready = sem("hots_ready")
        hots_used = sem("hots_used")
        half_summed = sem("half_summed")
        weight_copied = sem("weight_copied")
        title_summed = sem("title_summed")
        title_copied = sem("title_copied")
        title_folded = sem("title_folded")
        title_ready = sem("title_ready")
        piece_loaded = [sem(f"piece_loaded{i}") for i in range(SLOTS)]
        first_part_ready = sem("first_part_ready")
        second_part_ready = sem("second_part_ready")
        last_part_ready = sem("last_part_ready")
        own_rest = sem("own_rest")
        own_constants_loaded = sem("own_constants_loaded")
        orow_loaded = [sem(f"orow_loaded{s}") for s in range(2)]
        orow_free = sem("orow_free")
        q_step = sem("q_step")
        q_hot_ready = [sem(f"q_hot_ready{k}") for k in range(OWN)]
        candidates_summed = [sem(f"candidates_summed{k}") for k in range(OWN)]
        picked_ready = sem("picked_ready")
        looked_up = sem("looked_up")
        gathers_begun = sem("gathers_begun")
        gathered = [sem(f"gathered{s}") for s in range(2)]
        scaled_ready = sem("scaled_ready")
        sums_ready = sem("sums_ready")
        squared = sem("squared")
        transposed = sem("transposed")
        ones_ready = sem("ones_ready")
        xt_ready = sem("xt_ready")
        h1_summed = sem("h1_summed")
        h1_ready = sem("h1_ready")
        h2_summed = sem("h2_summed")
        h2_ready = sem("h2_ready")
        y_summed = sem("y_summed")
        deep_ready = sem("deep_ready")
        video_summed = sem("video_summed")
        video_ready = sem("video_ready")
        share_gathered = [sem(f"share_gathered{n}") for n in range(len(SHARES))]
        share_scaled = sem("share_scaled")
        share_transposed = sem("share_transposed")
        share_xt_ready = sem("share_xt_ready")
        last_h1_summed = sem("last_h1_summed")
        last_h1_ready = sem("last_h1_ready")
        last_h2_summed = sem("last_h2_summed")
        last_h2_ready = sem("last_h2_ready")
        last_y_summed = sem("last_y_summed")
        total_step = sem("total_step")
        out_written = sem("out_written")
        block = ctx.enter_context(nc.Block())

        @block.sync
        def _(sp):
            sp.dma_start(findex[:, 0:1, :], field_index[:, 0:1, :]).then_inc(first_index_loaded, 16)
            sp.dma_start(findex[:, 1:TILES, :], field_index[:, 1:TILES, :]).then_inc(index_loaded, 16)
            sp.dma_start(tindex[:], title_index).then_inc(words_loaded, 16)
            sp.dma_start(tvalue[:], title_value).then_inc(words_loaded, 16)
            sp.dma_start(wconst[:], word_constants).then_inc(words_loaded, 16)
            sp.dma_start(count16[:], counting_row).then_inc(words_loaded, 16)
            sp.dma_start(video_sb, video_t).then_inc(video_loaded, 16)
            sp.dma_start(vwt_sb[:], video_wt).then_inc(video_loaded, 16)
            sp.dma_start(vb_sb[VIDEO, :], video_b).then_inc(video_loaded, 16)

            def load_piece(n):
                k, a, b = PIECES[n]
                sp.dma_start(piece[n % SLOTS][:, 0:b - a, :],
                             own_table[:, k, a:b, :]).then_inc(piece_loaded[n % SLOTS], 16)

            def load_own_index(t, s):
                sp.dma_start(orow[s][:], own_index[:, :, bass.ds(t * P, P)].to_broadcast([P, OWN, P])
                             ).then_inc(orow_loaded[s], 16)

            sp.dma_start(ttable[:], title_table).then_inc(title_loaded, 16)
            sp.dma_start(fold_sb[:], fold).then_inc(title_loaded, 16)
            load_piece(0)
            load_piece(1)
            sp.dma_start(fvalue[:], field_value).then_inc(values_loaded, 16)
            sp.dma_start(ident[:], identity).then_inc(weights_loaded, 16)
            sp.dma_start(w1_sb[:, 0:KB - 1, :],
                         w1[0:(KB - 1) * P, :].rearrange("(k p) n -> p k n", p=P)).then_inc(weights_loaded, 16)
            sp.dma_start(w1_sb[0:FREST, KB - 1, :], w1[(KB - 1) * P:F * E, :]).then_inc(weights_loaded, 16)
            sp.dma_start(w1_sb[TITLE, KB - 1, :], w1[F * E:(F + 1) * E, :]).then_inc(weights_loaded, 16)
            sp.dma_start(w1_sb[VIDEO, KB - 1, :], w1[(F + 1) * E:(F + 2) * E, :]).then_inc(weights_loaded, 16)
            sp.dma_start(w2_sb[:], w2.rearrange("(k p) n -> p k n", p=P)).then_inc(weights_loaded, 16)
            sp.dma_start(b1_sb[:], b1).then_inc(weights_loaded, 16)
            sp.dma_start(b2_sb[:], b2).then_inc(weights_loaded, 16)
            sp.dma_start(bias_sb[:], bias.to_broadcast([P, 1])).then_inc(weights_loaded, 16)
            load_own_index(FIRST, 1)
            load_own_index(FIRST + 1, 0)
            sp.dma_start(q_of[:], q_constants).then_inc(own_constants_loaded, 16)
            sp.dma_start(cand_of[:], candidate_row).then_inc(own_constants_loaded, 16)
            for n in range(SLOTS, len(PIECES)):
                sp.wait_ge(last_part_ready, n - SLOTS + 1)
                load_piece(n)
            with sp.Fori(0, PAIRS - 3) as u:
                for s in range(2):
                    sp.wait_ge(q_step, 5 * (2 * u + s) + 2)
                    sp.sem_inc(orow_free, 1)
                    load_own_index(2 * u + s + FIRST + 2, 1 - s)
            sp.wait_ge(q_step, 5 * (TILES - 3 - FIRST) + 2)
            load_own_index(TILES - 1, 1)
            sp.wait_ge(total_step, 6)
            sp.dma_start(out, total[:]).then_inc(out_written, 16)
            sp.wait_ge(out_written, 16)

        WEIGHTS = 9 * 16

        @block.gpsimd
        def _(pool):
            def gather(s, f, arrived):
                pool.indirect_dma_start(
                    out=rows[s][:, f, :], out_offset=None, in_=table,
                    in_offset=bass.IndirectOffsetOnAxis(ap=fslot[s][:, f:f + 1], axis=0),
                ).then_inc(arrived, 16)

            for t in range(FIRST):
                pool.wait_ge(index_ready, t + 1)
                for f in range(F):
                    gather(t % 2, f, gathered[t % 2])
            with pool.Fori(0, (TILES - 1 - FIRST) // 2) as u:
                for s in range(2):
                    pool.wait_ge(index_ready, 2 * u + s + FIRST + 1)
                    pool.sem_inc(gathers_begun, 1)
                    for f in range(G):
                        gather(1 - s, f, gathered[1 - s])
            pool.wait_ge(index_ready, TILES)
            for n, (a, b) in enumerate(SHARES):
                for f in [f for f in range(a * FPB, min(b * FPB, F)) if f < G or f == LAST_G]:
                    gather(1, f, share_gathered[n])

        @block.vector
        def _(dve):
            def prepare(t, s):
                fi = findex[:, t, :]
                if not isinstance(t, int) or t > 0:
                    dve.wait_ge(index_ready, t)
                nc.vector.tensor_scalar(fneg[:], fi, 0, V, ALU.is_lt, ALU.mult).then_inc(index_step, 1)
                dve.wait_ge(index_step, 3 * t + 1)
                nc.vector.tensor_tensor(fslot[s][:], fneg[:], fi, ALU.add).then_inc(index_step, 1)
                dve.wait_ge(index_step, 3 * t + 2)
                nc.vector.tensor_scalar(fneg[:], fslot[s][:], 0, V - 1, ALU.max, ALU.min).then_inc(index_step, 1)
                dve.wait_ge(index_step, 3 * t + 3)
                nc.vector.tensor_tensor(fslot[s][:], fneg[:], fbase[:], ALU.add).then_inc(index_ready, 1)
                dve.wait_ge(index_ready, t + 1)
                nc.vector.tensor_scalar(ocand[s][:], fslot[s][:, G:F], CAND - 1, None, ALU.bitwise_and)

            def words(t):
                index, value = tindex[:, t, :], tvalue[:, t, :]
                column, minus = wconst[:, 0:1], [wconst[:, k:k + 1] for k in range(1, PARTS)]

                def twice(a):
                    return a.unsqueeze(2).to_broadcast([Q, GROUPS, 2])

                nc.vector.tensor_scalar(wneg[:], index, 0, VT, ALU.is_lt, ALU.mult)
                nc.vector.tensor_copy(wpart[0][:], value).then_inc(word_step, 1)
                dve.wait_ge(word_step, 5 * t + 1)
                nc.vector.tensor_tensor(wsum[:], wneg[:], index, ALU.add)
                nc.vector.scalar_tensor_tensor(wrest[0][:], wpart[0][:], minus[0], value, ALU.mult,
                                               ALU.add).then_inc(word_step, 1)
                dve.wait_ge(word_step, 5 * t + 2)
                nc.vector.tensor_scalar(wrow[:], wsum[:], 0, VT - 1, ALU.max, ALU.min)
                nc.vector.tensor_copy(wpart[1][:], wrest[0][:]).then_inc(word_step, 1)
                dve.wait_ge(word_step, 5 * t + 3)
                nc.vector.tensor_scalar(whi[:], wrow[:], LO_BITS, None, ALU.arith_shift_right)
                nc.vector.tensor_scalar(wlo[:], wrow[:], P - 1, None, ALU.bitwise_and)
                nc.vector.scalar_tensor_tensor(wrest[1][:], wpart[1][:], minus[1], wrest[0][:], ALU.mult,
                                               ALU.add).then_inc(word_step, 1)
                dve.wait_ge(word_step, 5 * t + 4)
                if not isinstance(t, int) or t > 0:
                    dve.wait_ge(hots_ready, t * CHUNKS)
                nc.vector.tensor_scalar(key2[:], twice(whi[:]), column, None, ALU.add)
                nc.vector.tensor_copy(lo2[:], twice(wlo[:]))
                nc.vector.tensor_copy(part2[:], twice(wrest[1][:])).then_inc(word_step, 1)
                dve.wait_ge(word_step, 5 * t + 5)

            def one_hots(t, chunks):
                def against(n):
                    return counting[:, 0:n].unsqueeze(1).to_broadcast([Q, GC, n]).rearrange("q g (n x) -> q g n x", x=2)

                def pairs(a, c, n):
                    return a[:, c * GC:(c + 1) * GC, :].unsqueeze(2).to_broadcast([Q, GC, n // 2, 2])

                def by_two(a):
                    return a[:].rearrange("q g (n x) -> q g n x", x=2)

                for c in chunks:
                    i = c % 2
                    dve.wait_ge(hots_used, t * CHUNKS + c + 1)
                    nc.vector.tensor_tensor(by_two(hi_hot[i]), against(W), pairs(key2, c, W),
                                            ALU.is_equal).then_inc(hi_hot_ready, 1)
                    nc.vector.tensor_tensor(by_two(lo_hot[c]), against(P), pairs(lo2, c, P), ALU.is_equal)
                    dve.wait_ge(hi_hot_ready, t * CHUNKS + c + 1)
                    nc.vector.tensor_tensor(by_two(hi_part[c]), by_two(hi_hot[i]), pairs(part2, c, W),
                                            ALU.mult).then_inc(hots_ready, 1)

            def subtract_first(n):
                k, a, b = PIECES[n]
                rest = piece[n % SLOTS][:, 0:b - a, :]
                dve.wait_ge(first_part_ready, n + 1)
                nc.vector.tensor_tensor(rest, rest, own_part[k][0][:, a:b, :], ALU.subtract).then_inc(own_rest, 1)

            def subtract_second(n):
                k, a, b = PIECES[n]
                dve.wait_ge(own_rest, n + 1)
                dve.wait_ge(second_part_ready, n + 1)
                nc.vector.tensor_tensor(own_part[k][2][:, a:b, :], piece[n % SLOTS][:, 0:b - a, :],
                                        own_part[k][1][:, a:b, :], ALU.subtract).then_inc(last_part_ready, 1)

            def own_rows(t, s, loads):
                dve.wait_ge(orow_loaded[s], loads * 16)
                index, done = orow[s][:], 5 * (t - FIRST)
                nc.vector.tensor_scalar(oneg[:], index, 0, V, ALU.is_lt, ALU.mult).then_inc(q_step, 1)
                dve.wait_ge(q_step, done + 1)
                nc.vector.tensor_tensor(osum[:], oneg[:], index, ALU.add).then_inc(q_step, 1)
                dve.wait_ge(q_step, done + 2)
                nc.vector.tensor_scalar(oclamped[:], osum[:], 0, V - 1, ALU.max, ALU.min).then_inc(q_step, 1)
                dve.wait_ge(q_step, done + 3)
                nc.vector.tensor_scalar(oq[:], oclamped[:], C_BITS, None, ALU.arith_shift_right).then_inc(q_step, 1)
                dve.wait_ge(q_step, done + 4)
                if not isinstance(t, int) or t > FIRST:
                    dve.wait_ge(q_hot_ready[OWN - 1], t - FIRST)
                nc.vector.tensor_copy(q_row[:], oq[:]).then_inc(q_step, 1)
                dve.wait_ge(q_step, done + 5)

            def own_one_hots(t, k):
                if not isinstance(t, int) or t > FIRST:
                    dve.wait_ge(candidates_summed[k], t - FIRST)
                nc.vector.tensor_tensor(q_hot[k][:].rearrange("p j (n x) -> p j n x", x=2),
                                        q_row[:, k, :].unsqueeze(1).to_broadcast([P, JS, P]).rearrange(
                                            "p j (n x) -> p j n x", x=2),
                                        q_of[:].unsqueeze(2).to_broadcast([P, JS, P // 2, 2]),
                                        ALU.is_equal).then_inc(q_hot_ready[k], 1)

            def look_up(t, s, k):
                done = OWN * (t - FIRST) + k
                dve.wait_ge(candidates_summed[k], t - FIRST + 1)
                dve.wait_ge(looked_up, done + 1)
                nc.vector.scalar_tensor_tensor(picked[:], cand_of[:], ocand[s][:, k:k + 1], pcand, ALU.is_equal,
                                               ALU.mult).then_inc(picked_ready, 1)
                dve.wait_ge(picked_ready, done + 2)
                nc.vector.tensor_reduce(rows[s][:, G + k, :], picked[:].rearrange("p (c e) -> p e c", e=EA),
                                        AXX, ALU.add).then_inc(looked_up, 1)

            def fields(u, s, prepared):
                t = 2 * u + s
                whole = 1 if s == 1 or (isinstance(u, int) and u == 0) else 2
                dve.wait_ge(gathered[s], G * 16 * u + (G + whole * OWN) * 16)
                if not isinstance(t, int) or t >= FIRST:
                    dve.wait_ge(looked_up, OWN * (t - FIRST + 1) + 1)
                dve.wait_ge(squared, t + 1)
                nc.vector.tensor_tensor(scaled[s][:].rearrange("p (f e) -> p f e", e=E), rows[s][:, :, 0:E],
                                        fvalue[:, t, :].unsqueeze(2).to_broadcast([P, F, E]), ALU.mult)
                nc.vector.tensor_tensor(weighted[:], rows[s][:, :, E], fvalue[:, t, :],
                                        ALU.mult).then_inc(scaled_ready, 1)
                dve.wait_ge(scaled_ready, t + 1)
                if prepared:
                    prepare(t + 2, s)
                nc.vector.tensor_reduce(first[:, bass.ds(t, 1)], weighted[:], AXX, ALU.add)
                nc.vector.tensor_reduce(fieldsum[s][:], scaled[s][:].rearrange("p (f e) -> p e f", e=E),
                                        AXX, ALU.add).then_inc(sums_ready, 1)
                dve.wait_ge(sums_ready, t + 1)

            def last_fields():
                t, s = TILES - 1, 1
                dve.wait_ge(looked_up, OWN * (t - FIRST + 1))
                dve.wait_ge(squared, t + 1)
                for n, (a, b) in enumerate(SHARES):
                    f, g = a * FPB, min(b * FPB, F)
                    dve.wait_ge(share_gathered[n], (g - f if f < G else 1) * 16)
                    nc.vector.tensor_tensor(scaled[s][:, f * E:g * E].rearrange("p (f e) -> p f e", e=E),
                                            rows[s][:, f:g, 0:E],
                                            fvalue[:, t, f:g].unsqueeze(2).to_broadcast([P, g - f, E]),
                                            ALU.mult).then_inc(share_scaled, 1)
                nc.vector.tensor_tensor(weighted[:], rows[s][:, :, E], fvalue[:, t, :],
                                        ALU.mult).then_inc(scaled_ready, 1)
                dve.wait_ge(scaled_ready, TILES)
                nc.vector.tensor_reduce(fieldsum[s][:], scaled[s][:].rearrange("p (f e) -> p e f", e=E),
                                        AXX, ALU.add).then_inc(sums_ready, 1)
                nc.vector.tensor_reduce(first[:, t:TILES], weighted[:], AXX, ALU.add).then_inc(total_step, 1)

            nc.vector.memset(ones[:], 1.0).then_inc(ones_ready, 1)
            dve.wait_ge(first_index_loaded, 32)
            prepare(0, 0)
            dve.wait_ge(index_loaded, 16)
            prepare(1, 1)
            dve.wait_ge(words_loaded, 64)
            nc.vector.tensor_copy(counting[:], count16[:]).then_inc(counting_ready, 1)
            dve.wait_ge(counting_ready, 1)
            words(0)
            one_hots(0, range(CHUNKS))
            subtract_first(0)
            subtract_first(1)
            subtract_second(0)
            words(1)
            subtract_second(1)
            one_hots(1, range(AHEAD))
            dve.wait_ge(values_loaded, 16)
            dve.wait_ge(own_constants_loaded, 32)
            for t in range(2):
                fields(0, t, prepared=True)
                one_hots(t + 1, [2])
                subtract_first(2 * t + 2)
                subtract_first(2 * t + 3)
                one_hots(t + 1, [3])
                subtract_second(2 * t + 2)
                subtract_second(2 * t + 3)
                words(t + 2)
                if t + 2 == FIRST:
                    own_rows(FIRST, 1, 1)
                one_hots(t + 2, [0])
                if t + 2 == FIRST:
                    own_one_hots(FIRST, 0)
                one_hots(t + 2, [1])
                if t + 2 == FIRST:
                    own_one_hots(FIRST, 1)
            with dve.Fori(1, PAIRS - 1) as u:
                for s in range(2):
                    t = 2 * u + s
                    fields(u, s, prepared=True)
                    one_hots(t + 1, [2])
                    look_up(t + 1, 1 - s, 0)
                    one_hots(t + 1, [3])
                    words(t + 2)
                    own_rows(t + 2, s, u + s)
                    one_hots(t + 2, [0])
                    own_one_hots(t + 2, 0)
                    look_up(t + 1, 1 - s, 1)
                    one_hots(t + 2, [1])
                    own_one_hots(t + 2, 1)
            fields(PAIRS - 1, 0, prepared=False)
            one_hots(TILES - 1, [2])
            look_up(TILES - 1, 1, 0)
            one_hots(TILES - 1, [3])
            last_fields()
            dve.wait_ge(squared, TILES + 2)
            dve.wait_ge(weights_loaded, WEIGHTS)
            nc.vector.tensor_tensor(sum_of_sq[:, TILES - 1:TILES], sum_of_sq[:, TILES - 1:TILES], early_squares[:],
                                    ALU.add).then_inc(total_step, 1)
            dve.wait_ge(total_step, 2)
            nc.vector.tensor_tensor(diff[:], sq_of_sum[:], sum_of_sq[:], ALU.subtract).then_inc(total_step, 1)
            dve.wait_ge(total_step, 3)
            nc.vector.tensor_scalar(diff[:], diff[:], 0.5, bias_sb[:], ALU.mult, ALU.add).then_inc(total_step, 1)
            dve.wait_ge(total_step, 4)
            nc.vector.tensor_tensor(linear[:], first[:], diff[:], ALU.add).then_inc(total_step, 1)
            dve.wait_ge(total_step, 5)
            dve.wait_ge(deep_ready, TILES)
            nc.vector.tensor_tensor(total[:, 0:TILES - 1], linear[:, 0:TILES - 1], deep[:, 0:TILES - 1], ALU.add)
            dve.wait_ge(last_y_summed, 1)
            nc.vector.tensor_tensor(total[:, TILES - 1:TILES], linear[:, TILES - 1:TILES], py,
                                    ALU.add).then_inc(total_step, 1)

        @block.tensor
        def _(pe):
            def products(t, c):
                pe.wait_ge(hots_ready, t * CHUNKS + c + 1)
                for g in range(GC):
                    if g % (2 * GB) == 0:
                        pe.wait_ge(weight_copied, (t * CHUNKS + c) * (BANKS // 2) + g // (2 * GB) + 1)
                    last = nc.tensor.matmul(pw[:, g // GB, g % GB * W:(g % GB + 1) * W], lo_hot[c][:, g, :],
                                            hi_part[c][:, g, :], start=True, stop=True)
                    if g == 2 * GB - 1:
                        last.then_inc(half_summed, 1)
                last.then_inc(hots_used, 1)

            def title(t):
                pe.wait_ge(weight_copied, (t * CHUNKS + CHUNKS) * (BANKS // 2) + BANKS // 2)
                for h in range(HI):
                    g = h % FPB
                    last = nc.tensor.matmul(ptitle[g * E:(g + 1) * E, :], ttable[:, h, :],
                                            weight[:, h, :], start=(h < FPB), stop=(h >= HI - FPB))
                last.then_inc(title_summed, 1)

            def fold_title(t):
                pe.wait_ge(title_copied, t + 1)
                nc.tensor.matmul(ptitle[TITLE, :], fold_sb[:], title_sums[:], start=True,
                                 stop=True).then_inc(title_folded, 1)

            def candidates(t, k, js):
                if js[0] == 0:
                    pe.wait_ge(q_hot_ready[k], t - FIRST + 1)
                    pe.wait_ge(picked_ready, OWN * (t - FIRST) + k + 1)
                for j in js:
                    for part in range(PARTS):
                        last = nc.tensor.matmul(pcand, q_hot[k][:, j, :], own_part[k][part][:, j, :],
                                                start=(j == 0 and part == 0), stop=(j == JS - 1 and part == PARTS - 1))
                if js[-1] == JS - 1:
                    last.then_inc(candidates_summed[k], 1)

            def share_transposes(n):
                pe.wait_ge(share_scaled, n + 1)
                a, b = SHARES[n]
                for k in range(a, b):
                    w = min(P, F * E - P * k)
                    last = nc.tensor.transpose(share_pt[n][0:w, k - a, :], scaled[1][:, P * k:P * k + w], ident[:])
                last.then_inc(share_transposed, 1)

            def share_first_layer(blocks, end=False):
                for m in range(KH):
                    for k in blocks:
                        last = nc.tensor.matmul(last_ph1[m], w1_sb[:, k, m * P:(m + 1) * P], xt[1][:, k, :],
                                                start=(k == 0), stop=end)
                    if end:
                        last.then_inc(last_h1_summed, 1)

            def tile(u, s):
                t = 2 * u + s
                own = not isinstance(t, int) or t + 1 >= FIRST
                before_last = isinstance(t, int) and t == TILES - 2
                products(t + 1, 0)
                if own:
                    candidates(t + 1, 0, A_STAGES[0])
                products(t + 1, 1)
                pe.wait_ge(scaled_ready, t + 1)
                pe.wait_ge(title_ready, t + 1)
                for k in range(KB):
                    n = min(P, F * E - P * k)
                    last = nc.tensor.transpose(pt[k // FPB][0:n, k % FPB, :], scaled[s][:, P * k:P * k + n], ident[:])
                    if k in (FPB - 1, KB - 1):
                        last.then_inc(transposed, 1)
                if own:
                    candidates(t + 1, 0, A_STAGES[1])
                pe.wait_ge(xt_ready, 2 * t + 2)
                for m in range(KH):
                    for k in range(KB):
                        last = nc.tensor.matmul(ph1[:, m, :], w1_sb[:, k, m * P:(m + 1) * P], xt[s][:, k, :],
                                                start=(k == 0), stop=(k == KB - 1))
                last.then_inc(h1_summed, 1)
                products(t + 1, 2)
                if own and not before_last:
                    candidates(t + 1, 1, range(JS))
                products(t + 1, 3)
                pe.wait_ge(h1_ready, t + 1)
                pe.wait_ge(deep_ready, t + 1)
                for m in range(K2):
                    for k in range(KH):
                        last = nc.tensor.matmul(ph2[:, m, :], w2_sb[:, k, m * P:(m + 1) * P], h1[s][:, k, :],
                                                start=(k == 0), stop=(k == KH - 1))
                last.then_inc(h2_summed, 1)
                if before_last:
                    share_transposes(0)
                    share_transposes(1)
                title(t + 1)
                pe.wait_ge(h2_ready, t + 1)
                for m in range(K2):
                    last = nc.tensor.matmul(py, h2[s][:, m, :], ones[:], start=(m == 0), stop=(m == K2 - 1))
                last.then_inc(y_summed, 1)
                if before_last:
                    pe.wait_ge(share_xt_ready, 1)
                else:
                    fold_title(t + 1)

            def last_tile():
                s = 1
                share_first_layer(range(0, FPB // 2))
                fold_title(TILES - 1)
                share_first_layer(range(FPB // 2, FPB))
                pe.wait_ge(title_ready, TILES)
                for n, (a, b) in enumerate(SHARES[1:], 1):
                    if n + 1 < len(SHARES):
                        share_transposes(n + 1)
                    pe.wait_ge(share_xt_ready, n + 1)
                    share_first_layer(range(a, b), end=(n == len(SHARES) - 1))
                for k in range(KH):
                    pe.wait_ge(last_h1_ready, k + 1)
                    for m in range(K2):
                        last = nc.tensor.matmul(last_ph2[m], w2_sb[:, k, m * P:(m + 1) * P], h1[s][:, k, :],
                                                start=(k == 0), stop=(k == KH - 1))
                        if k == KH - 1:
                            last.then_inc(last_h2_summed, 1)
                for m in range(K2):
                    pe.wait_ge(last_h2_ready, m + 1)
                    last = nc.tensor.matmul(py, h2[s][:, m, :], ones[:], start=(m == 0), stop=(m == K2 - 1))
                last.then_inc(last_y_summed, 1)

            pe.wait_ge(video_loaded, 48)
            for c in range(B // VCHUNK):
                nc.tensor.matmul(pw[VIDEO, c, :], vwt_sb[:], video_sb[:, c * VCHUNK:(c + 1) * VCHUNK],
                                 start=True, stop=True).then_inc(video_summed, 1)
            pe.wait_ge(title_loaded, 32)
            pe.wait_ge(video_ready, B // VCHUNK)
            for c in range(CHUNKS):
                products(0, c)
            title(0)
            fold_title(0)
            pe.wait_ge(weights_loaded, WEIGHTS)
            pe.wait_ge(ones_ready, 1)
            tile(0, 0)
            tile(0, 1)
            pe.wait_ge(last_part_ready, len(PIECES))
            with pe.Fori(1, PAIRS - 1) as u:
                for s in range(2):
                    tile(u, s)
            tile(PAIRS - 1, 0)
            last_tile()

        @block.scalar
        def _(act):
            def weights(t, c):
                for half in range(2):
                    if half == 0:
                        act.wait_ge(half_summed, t * CHUNKS + c + 1)
                    else:
                        act.wait_ge(hots_used, t * CHUNKS + c + 1 + CHUNKS)
                    n = GB * GI
                    first_item = (c * GC + half * 2 * GB) * GI
                    nc.scalar.activation(
                        weight[:, :, first_item:first_item + 2 * n].rearrange("p h (b i) -> p b h i", i=n),
                        pw[:, 2 * half:2 * half + 2, 0:GB * W].rearrange("p b (i h) -> p b h i", h=HI),
                        ACT.Copy).then_inc(weight_copied, 1)

            def title(t, s):
                act.wait_ge(title_summed, t + 1)
                nc.scalar.activation(title_sums[:], ptitle, ACT.Copy).then_inc(title_copied, 1)
                act.wait_ge(title_folded, t + 1)
                nc.scalar.activation(xt[s][TITLE, KB - 1, :], ptitle[TITLE, :], ACT.Copy).then_inc(title_ready, 1)

            def first_part(n):
                k, a, b = PIECES[n]
                act.wait_ge(piece_loaded[n % SLOTS], (n // SLOTS + 1) * 16)
                nc.scalar.activation(own_part[k][0][:, a:b, :], piece[n % SLOTS][:, 0:b - a, :],
                                     ACT.Copy).then_inc(first_part_ready, 1)

            def second_part(n):
                k, a, b = PIECES[n]
                act.wait_ge(own_rest, n + 1)
                nc.scalar.activation(own_part[k][1][:, a:b, :], piece[n % SLOTS][:, 0:b - a, :],
                                     ACT.Copy).then_inc(second_part_ready, 1)

            def copy_share(n):
                act.wait_ge(share_transposed, n + 1)
                a, b = SHARES[n]
                w = FREST if b == KB else P
                nc.scalar.activation(xt[1][0:w, a:b, :], share_pt[n][0:w, 0:b - a, :],
                                     ACT.Copy).then_inc(share_xt_ready, 1)

            def tile(u, s):
                t = 2 * u + s
                for c in range(AHEAD):
                    weights(t + 1, c)
                act.wait_ge(transposed, 2 * t + 1)
                nc.scalar.activation(xt[s][:, 0:FPB, :], pt[0][:], ACT.Copy).then_inc(xt_ready, 1)
                act.wait_ge(transposed, 2 * t + 2)
                nc.scalar.activation(xt[s][VIDEO, KB - 1, :], video_emb[VIDEO, bass.ds(t * P, P)], ACT.Copy)
                nc.scalar.activation(xt[s][0:FREST, KB - 1, :], pt[1][0:FREST, KB - 1 - FPB, :], ACT.Copy)
                nc.scalar.activation(xt[s][:, FPB:KB - 1, :], pt[1][:, 0:KB - 1 - FPB, :],
                                     ACT.Copy).then_inc(xt_ready, 1)
                act.wait_ge(sums_ready, t + 1)
                nc.scalar.activation(square[:], scaled[s][:], ACT.Square, accum_out=sum_of_sq[:, bass.ds(t, 1)])
                nc.scalar.activation(square_s[:], fieldsum[s][:], ACT.Square,
                                     accum_out=sq_of_sum[:, bass.ds(t, 1)]).then_inc(squared, 1)
                if isinstance(t, int) and t < 2:
                    first_part(2 * t + 2)
                    first_part(2 * t + 3)
                    second_part(2 * t + 2)
                    second_part(2 * t + 3)
                act.wait_ge(h1_summed, t + 1)
                for m in range(KH):
                    last = nc.scalar.activation(h1[s][:, m, :], ph1[:, m, :], ACT.Relu, bias=b1_sb[:, m:m + 1])
                last.then_inc(h1_ready, 1)
                weights(t + 1, 2)
                weights(t + 1, 3)
                act.wait_ge(h2_summed, t + 1)
                for m in range(K2):
                    last = nc.scalar.activation(h2[s][:, m, :], ph2[:, m, :], ACT.Relu, bias=b2_sb[:, m:m + 1])
                last.then_inc(h2_ready, 1)
                if isinstance(t, int) and t == TILES - 2:
                    copy_share(0)
                    copy_share(1)
                    nc.scalar.activation(xt[1][VIDEO, KB - 1, :], video_emb[VIDEO, (TILES - 1) * P:B], ACT.Copy)
                title(t + 1, 1 - s)
                act.wait_ge(y_summed, t + 1)
                nc.scalar.activation(deep[:, bass.ds(t, 1)], py, ACT.Copy).then_inc(deep_ready, 1)

            def last_tile():
                t, s = TILES - 1, 1
                for n in range(2, len(SHARES)):
                    copy_share(n)
                    if n == 2:
                        early = SHARES[n][1] * P
                        nc.scalar.activation(square[:, 0:early], scaled[s][:, 0:early], ACT.Square,
                                             accum_out=early_squares[:])
                for m in range(KH):
                    act.wait_ge(last_h1_summed, m + 1)
                    nc.scalar.activation(h1[s][:, m, :], last_ph1[m], ACT.Relu,
                                         bias=b1_sb[:, m:m + 1]).then_inc(last_h1_ready, 1)
                act.wait_ge(sums_ready, TILES)
                nc.scalar.activation(square[:, early:], scaled[s][:, early:], ACT.Square,
                                     accum_out=sum_of_sq[:, t:TILES])
                nc.scalar.activation(square_s[:], fieldsum[s][:], ACT.Square,
                                     accum_out=sq_of_sum[:, t:TILES]).then_inc(squared, 1)
                for m in range(K2):
                    act.wait_ge(last_h2_summed, m + 1)
                    nc.scalar.activation(h2[s][:, m, :], last_ph2[m], ACT.Relu,
                                         bias=b2_sb[:, m:m + 1]).then_inc(last_h2_ready, 1)

            act.dma_start(fbase[:], field_base).then_inc(first_index_loaded, 16)
            act.sem_inc(squared, 2)
            act.sem_inc(picked_ready, 1)
            act.sem_inc(looked_up, 1)
            act.sem_inc(deep_ready, 1)
            act.sem_inc(hots_used, CHUNKS)
            act.sem_inc(weight_copied, BANKS // 2)
            act.wait_ge(video_loaded, 48)
            for c in range(B // VCHUNK):
                act.wait_ge(video_summed, c + 1)
                nc.scalar.activation(video_emb[VIDEO, c * VCHUNK:(c + 1) * VCHUNK], pw[VIDEO, c, :],
                                     ACT.Identity, bias=vb_sb[VIDEO, :]).then_inc(video_ready, 1)
            act.wait_ge(video_ready, B // VCHUNK)
            first_part(0)
            for c in range(CHUNKS):
                if c == 2:
                    first_part(1)
                weights(0, c)
            second_part(0)
            second_part(1)
            title(0, 0)
            act.wait_ge(weights_loaded, WEIGHTS)
            tile(0, 0)
            tile(0, 1)
            with act.Fori(1, PAIRS - 1) as u:
                for s in range(2):
                    tile(u, s)
            tile(PAIRS - 1, 0)
            last_tile()


def kernel(r_Xi, r_title_feature, L0_rec_Xv, L0_rec_video_feature, L0_rec_title_value, L0_rec_first_tables,
           L0_rec_second_tables, L0_rec_title_table, L0_rec_video_W, L0_rec_video_b, L0_rec_W1, L0_rec_b1,
           L0_rec_W2, L0_rec_b2, L0_rec_bias):
    import numpy as np
    import concourse.bacc as bacc
    from concourse.bass_utils import run_bass_kernel_spmd

    def tiles(a):
        return np.ascontiguousarray(np.asarray(a).reshape(TILES, P, -1).transpose(1, 0, 2))

    def word_groups(a):
        one = np.asarray(a).reshape(TILES, GROUPS, GI * L).transpose(2, 0, 1)
        return np.ascontiguousarray(np.concatenate([one] * PARTS, axis=0))

    c = np.ascontiguousarray
    table = np.concatenate([np.asarray(L0_rec_second_tables), np.asarray(L0_rec_first_tables)[:, :, None]], axis=2)
    rows = np.zeros((F, VP, EA), np.float32)
    rows[:, :V] = table
    own = np.zeros((OWN, JS * P * CAND, EA), np.float32)
    own[:, :V] = table[G:]
    title = np.zeros((HI * P, E), np.float32)
    title[:VT] = np.asarray(L0_rec_title_table)
    w1 = np.asarray(L0_rec_W1)
    q = np.arange(Q)
    arrays = {
        "table": rows.reshape(F * VP, EA),
        "own_table": c(own.reshape(OWN, JS, P, CW).transpose(2, 0, 1, 3)),
        "own_index": c(np.asarray(r_Xi)[:, G:, 0].T.reshape(1, OWN, B)),
        "title_table": c(title.reshape(HI, P, E).transpose(1, 0, 2)),
        "field_index": tiles(np.asarray(r_Xi)[:, :, 0]),
        "field_value": tiles(L0_rec_Xv),
        "title_index": word_groups(r_title_feature),
        "title_value": word_groups(L0_rec_title_value),
        "video_t": c(np.asarray(L0_rec_video_feature).T),
        "video_wt": c(np.asarray(L0_rec_video_W).T),
        "video_b": c(np.asarray(L0_rec_video_b).reshape(E, 1)),
        "w1": c(w1),
        "b1": c(np.asarray(L0_rec_b1).reshape(KH, P).T),
        "w2": c(L0_rec_W2),
        "b2": c(np.asarray(L0_rec_b2).reshape(K2, P).T),
        "bias": c(np.asarray(L0_rec_bias).reshape(1, 1)),
        "field_base": c(np.broadcast_to(np.arange(F, dtype=np.int32) * VP, (P, F))),
        "word_constants": c(np.stack([q // L % GI * HI] + [-(q // (GI * L) >= k).astype(np.float32)
                                                      for k in range(1, PARTS)], axis=1).astype(np.float32)),
        "counting": c(np.broadcast_to(np.arange(P, dtype=np.int16), (Q, P))),
        "q_constants": c(np.broadcast_to((np.arange(JS) * P + np.arange(P)[:, None]).astype(np.int16)[:, :, None],
                                         (P, JS, 2))),
        "candidate_row": c(np.broadcast_to(np.repeat(np.arange(CAND, dtype=np.float32), EA), (P, CW))),
        "identity": np.eye(P, dtype=np.float32),
        "fold": c(np.tile(np.eye(E, dtype=np.float32), (FPB, 1))),
    }
    nc = bacc.Bacc("TRN2", target_bir_lowering=False, num_devices=1)
    args = [nc.dram_tensor(f"in_{k}", a.shape, mybir.dt.from_np(a.dtype), kind="ExternalInput").ap()
            for k, a in arrays.items()]
    out = nc.dram_tensor("out", (P, TILES), mybir.dt.float32, kind="ExternalOutput").ap()
    build(nc, *args, out)
    r = run_bass_kernel_spmd(nc, [{f"in_{k}": a for k, a in arrays.items()}], core_ids=[0])
    return np.asarray(r.results[0]["out"]).T.reshape(B)
```
